# Optimizing a Trainium2 kernel written in Bass

```python
import numpy as np
import jax
import jax.numpy as jnp

def _softmax(x, axis=-1):
    return jax.nn.softmax(x, axis=axis)

def _gelu(x):
    return jax.nn.gelu(x, approximate=True)

def _silu(x):
    return jax.nn.silu(x)

def _sigmoid(x):
    return jax.nn.sigmoid(x)

def _layernorm(x, axis=-1, eps=1e-05):
    m = jnp.mean(x, axis=axis, keepdims=True)
    v = jnp.var(x, axis=axis, keepdims=True)
    return (x - m) / jnp.sqrt(v + eps)

def _scatter_add(tgt, idx, src, axis=0):
    return tgt.at[idx].add(src)

def _segment_sum(src, seg, n):
    return jax.ops.segment_sum(src, seg, n)
kernel_name = 'mk_adj_resnorm_d2_adj_r2_97d3ad'

def setup_inputs(seed: int=0):
    np.random.seed(seed)
    _w = jnp.asarray

    def _rec_inputs():
        import jax
        import jax.numpy as jnp
        _gk = jax.random.key(seed)
        x = -0.001003 + 1 * jax.random.normal(jax.random.fold_in(_gk, 1), (4096, 128), jnp.float32)
        _a = jax.random.bernoulli(jax.random.fold_in(_gk, 2), 0.000976562, (4096, 4096))
        _a = jnp.logical_or(_a, jnp.swapaxes(_a, -1, -2))
        _a = jnp.logical_or(_a, jnp.eye(4096, dtype=bool))
        _af = _a.astype(jnp.float32)
        _af = _af * jax.random.uniform(jax.random.fold_in(_gk, 3), (4096, 4096), jnp.float32, 0.05, 0.999999)
        adj = _af
        return (x, adj)
    x, adj = _rec_inputs()

    def _L0_gnn_setup():
        import jax, jax.numpy as jnp
        import numpy as np
        N = 3072
        HID = 128
        T = 350
        DENSITY = 0.05
        key = jax.random.key(seed)
        k1, k2, k3, k4, k5, k6 = jax.random.split(key, 6)
        h = jax.random.normal(k1, (N, HID), dtype=jnp.float32)
        a = jax.random.uniform(k2, (N, N), dtype=jnp.float32)
        mask = jax.random.uniform(k3, (N, N)) < DENSITY
        adj = jnp.where(mask, a, 0.0)
        simlar = jax.random.normal(k4, (N, N), dtype=jnp.float32)
        s = 1.0 / np.sqrt(HID)
        W_proj = jax.random.uniform(k5, (HID, HID), minval=-s, maxval=s, dtype=jnp.float32)
        b_proj = jnp.zeros((HID,), dtype=jnp.float32)
        W_gcn = jax.random.uniform(k6, (HID, HID), minval=-s, maxval=s, dtype=jnp.float32)
        b_gcn = jnp.zeros((HID,), dtype=jnp.float32)
        return {'h': h, 'adj': adj, 'simlar': simlar, 'W_proj': W_proj, 'b_proj': b_proj, 'W_gcn': W_gcn, 'b_gcn': b_gcn}
    _L0_gnn_all = _L0_gnn_setup()
    _L0_gnn_in = {k: v for k, v in _L0_gnn_all.items() if k in ('W_proj', 'b_proj', 'W_gcn', 'b_gcn')}
    del _L0_gnn_all

    def _L1_gnn_setup():
        import jax, jax.numpy as jnp
        import numpy as np
        N = 4096
        IN_F = 128
        OUT_F = 128
        key = jax.random.key(seed)
        ks = jax.random.split(key, 7)
        feats = jax.random.normal(ks[0], (N, IN_F), dtype=jnp.float32)
        node_adj = jax.random.normal(ks[1], (N, N), dtype=jnp.float32)
        edge_adj = jax.random.normal(ks[2], (N, N), dtype=jnp.float32)
        node_weight = jax.random.normal(ks[3], (2 * IN_F, OUT_F), dtype=jnp.float32) * 0.05
        node_bias = jax.random.normal(ks[4], (OUT_F,), dtype=jnp.float32) * 0.05
        edge_weight = jax.random.normal(ks[5], (IN_F, OUT_F), dtype=jnp.float32) * 0.05
        edge_bias = jax.random.normal(ks[6], (OUT_F,), dtype=jnp.float32) * 0.05
        return {'feats': feats, 'node_adj': node_adj, 'edge_adj': edge_adj, 'node_weight': node_weight, 'node_bias': node_bias, 'edge_weight': edge_weight, 'edge_bias': edge_bias}
    _L1_gnn_all = _L1_gnn_setup()
    _L1_gnn_in = {k: v for k, v in _L1_gnn_all.items() if k in ('node_weight', 'node_bias', 'edge_weight', 'edge_bias')}
    del _L1_gnn_all
    return {'x': x, 'adj': adj, 'L0_gnn_W_proj': _L0_gnn_in['W_proj'], 'L0_gnn_b_proj': _L0_gnn_in['b_proj'], 'L0_gnn_W_gcn': _L0_gnn_in['W_gcn'], 'L0_gnn_b_gcn': _L0_gnn_in['b_gcn'], 'L1_gnn_node_weight': _L1_gnn_in['node_weight'], 'L1_gnn_node_bias': _L1_gnn_in['node_bias'], 'L1_gnn_edge_weight': _L1_gnn_in['edge_weight'], 'L1_gnn_edge_bias': _L1_gnn_in['edge_bias']}

def reference(x, adj, L0_gnn_W_proj, L0_gnn_b_proj, L0_gnn_W_gcn, L0_gnn_b_gcn, L1_gnn_node_weight, L1_gnn_node_bias, L1_gnn_edge_weight, L1_gnn_edge_bias):
    import jax
    import jax.numpy as jnp

    def _L0_gnn_ref(h, adj, simlar, W_proj, b_proj, W_gcn, b_gcn):
        import jax, jax.numpy as jnp
        import numpy as np
        N = 3072
        HID = 128
        T = 350
        DENSITY = 0.05
        sim = jnp.tanh(adj * simlar)
        filt = sim * (adj > 0).astype(sim.dtype)
        vals, idx = jax.lax.top_k(filt, T)
        nnz = jnp.sum(filt != 0, axis=1)
        keep = jnp.arange(T)[None, :] < nnz[:, None]
        rows = jnp.arange(filt.shape[0])[:, None]
        new_adj = jnp.zeros_like(filt).at[rows, idx].set(jnp.where(keep, vals, 0.0))
        h2 = jnp.tanh(h @ W_proj + b_proj)
        feat = jax.nn.relu(new_adj @ (h2 @ W_gcn) + b_gcn)
        return feat

    def _L1_gnn_ref(feats, node_adj, edge_adj, node_weight, node_bias, edge_weight, edge_bias):
        import jax, jax.numpy as jnp
        import numpy as np
        N = 4096
        IN_F = 128
        OUT_F = 128
        pos = jnp.matmul((node_adj > 0).astype(feats.dtype), feats)
        neg = jnp.matmul((node_adj < 0).astype(feats.dtype), feats)
        node_support = jnp.concatenate([pos, neg], axis=1)
        node_output = jnp.matmul(node_support, node_weight)
        node_output = node_output + node_bias * jnp.diagonal(edge_adj)[:, None]
        edge_support = jnp.matmul(edge_adj, feats)
        edge_output = jnp.matmul(edge_support, edge_weight)
        edge_output = edge_output + edge_bias * jnp.diagonal(node_adj)[:, None]
        return node_output + edge_output
    x = _layernorm(x + _L0_gnn_ref(x, adj, adj, L0_gnn_W_proj, L0_gnn_b_proj, L0_gnn_W_gcn, L0_gnn_b_gcn), axis=-1)
    x = _layernorm(x + _L1_gnn_ref(x, adj, adj, L1_gnn_node_weight, L1_gnn_node_bias, L1_gnn_edge_weight, L1_gnn_edge_bias), axis=-1)
    return x

_drawn_inputs = setup_inputs


def setup_inputs(seed=0):
    import zlib

    import numpy as np

    out = dict(_drawn_inputs(seed))
    spreads = {'L0_gnn_b_proj': (0.0, 0.1), 'L0_gnn_b_gcn': (0.0, 0.1)}
    factors = {'L1_gnn_node_bias': 4.151, 'L1_gnn_edge_bias': 3.981}
    for name, (base, spread) in spreads.items():
        noise = np.random.default_rng([zlib.crc32(name.encode()), seed]).standard_normal(out[name].shape)
        drawn = base * np.exp(spread * noise) if base else spread * noise
        out[name] = jnp.asarray(drawn.astype(out[name].dtype))
    for name, factor in factors.items():
        out[name] = (out[name] * factor).astype(out[name].dtype)
    return out
```

```python
import concourse.bass as bass
from concourse import mybir
from concourse.alu_op_type import AluOpType as ALU
from contextlib import ExitStack
import numpy as np


P = 128
SQ = 32
F = 128
TOP = 350
EPS = 1e-5
MAX8 = 8
RSQRT_SEED = 0x5F3759DF
NEWTON = 3
LN_STEPS = 7 + 3 * NEWTON


def build(nc, x, adj, w_proj, b_proj, w_gcn, b_gcn, node_w, node_b, edge_w, edge_b, out):
    f32, f32r, i32 = mybir.dt.float32, mybir.dt.float32r, mybir.dt.int32
    ACT = mybir.ActivationFunctionType

    N = adj.shape[0]
    QUARTERS = P // SQ
    QUARTER = N // QUARTERS
    BLOCKS = N // P
    CH = 512
    CHUNKS = N // CH
    ROWSETS = CH // SQ
    TILES = CH // P
    ALL_TILES = N // P
    PIECES = 4
    PCOLS = QUARTER // PIECES
    HALVES = 2
    HB = PCOLS // HALVES // SQ
    SLOTS = 4
    HSLOTS = 4
    HPC = PIECES * HALVES
    LAST = (CHUNKS - 1, CHUNKS // 2 - 1, 1)
    SQ_POOL = HB // 2

    ctx = ExitStack()
    with ctx:
        def sb(name, shape, dt=f32):
            return ctx.enter_context(nc.sbuf_tensor(name, shape, dt))

        def pb(name, shape):
            return ctx.enter_context(nc.psum_tensor(name, shape, f32))

        def sem(name):
            return ctx.enter_context(nc.semaphore(name))

        shared_at = -(-nc.sbuf_base // SQ) * SQ
        sb("shared", [P, HSLOTS * HB * CH])
        masks = nc.alloc_sbuf_tensor_at("masks", [P, HSLOTS, HB, CH], f32r, offset=shared_at)
        early = nc.alloc_sbuf_tensor_at("early", [P, 2, N], f32, offset=shared_at)
        a_rows = sb("a_rows", [P, SLOTS, ROWSETS, PCOLS])
        a_cols = sb("a_cols", [P, HSLOTS, HB, CH])
        feat_t = sb("feat_t", [P, N])
        rhs = sb("rhs", [P, BLOCKS, F])
        pos_hi = sb("pos_hi", [P, BLOCKS, F], f32r)
        pos_lo = sb("pos_lo", [P, BLOCKS, F], f32r)
        z_t = sb("z_t", [P, CH])
        y_rows = sb("y_rows", [P, TILES, F])
        n_rows = sb("n_rows", [P, 2, TILES, F])
        w_pg = sb("w_pg", [P, 2, F])
        w_pne = sb("w_pne", [P, 3, F])
        b_col = sb("b_col", [P, 2])
        b_row = sb("b_row", [1, 3, F])
        bias_bc = sb("bias_bc", [P, 2, F])
        diag = sb("diag", [P, ALL_TILES])
        ident = sb("ident", [P, P])
        ones = sb("ones", [P, P])
        bn = sb("bn", [P, TILES, 6])
        mean = sb("mean", [P, TILES])
        var = sb("var", [P, TILES])
        root = sb("root", [P, TILES])
        tmp = sb("tmp", [P, TILES])
        signs = sb("signs", [P, CHUNKS * PIECES])
        negs = sb("negs", [P, CHUNKS * PIECES])
        chunk_signs = sb("chunk_signs", [P, CHUNKS])
        over = sb("over", [P, CHUNKS])
        fails = sb("fails", [P, 2])
        flag = sb("flag", [1, 1], i32)
        top8 = sb("top8", [P, MAX8])
        held_at = sb("held_at", [P, 2])

        acc = [pb(f"acc{k}", [P, CH]) for k in range(2)]
        to_rows = pb("to_rows", [P, TILES, F])
        to_cols = pb("to_cols", [P, CH])
        stage = [pb(f"stage{k}", [P, CH]) for k in range(4)]

        def half_in(slot, h):
            w = PCOLS // HALVES
            return a_rows[:, slot, :, h * w:(h + 1) * w].rearrange("p r (b j) -> p r b j", j=SQ)

        def half_out(hs):
            return a_cols[:, hs, :, :].rearrange("p b (r i) -> p r b i", i=SQ)

        def blk(t, b):
            return t[:, b * P:(b + 1) * P]

        def nodes(t, q, parity):
            t = t.rearrange("f (b q j) -> f q b j", q=QUARTERS, j=SQ)
            return t[:, q, parity * ROWSETS:(parity + 1) * ROWSETS, :]

        def sets(t):
            return t[:].rearrange("f (b j) -> f b j", j=SQ)

        xr = early[:, 1, :].rearrange("p (t f) -> p t f", f=F)
        h_t = early[:, 0, :]

        def row(k):
            return a_rows[:, k, :, :].rearrange("p r c -> p (r c)")

        g_in, g_work, g_kept = row(0), row(1), row(2)
        g_small = row(3).rearrange("p (k f) -> p k f", f=F)
        g_pick, g_cols, g_gt, g_lt, g_sum, g_x, g_y = (g_small[:, k, :] for k in range(7))
        g_out = n_rows[:, 0, 0, :]
        g_pos = a_cols[:, 0:2, :, :].rearrange("p s b c -> p (s b c)").rearrange("p (b f) -> p b f", f=F)
        g_neg = a_cols[:, 2:4, :, :].rearrange("p s b c -> p (s b c)").rearrange("p (b f) -> p b f", f=F)

        def g_blk(t):
            return t.rearrange("p (q b j) -> p b q j", q=QUARTERS, j=SQ)

        def g_nodes(q, s):
            t = feat_t[:].rearrange("f (b q j) -> f q b j", q=QUARTERS, j=SQ)
            return t[:, q, bass.ds(s * QUARTERS, QUARTERS), :]

        x_loaded = [sem(f"x_loaded{g}") for g in range(CHUNKS)]
        small_loaded = sem("small_loaded")
        wl1_loaded = sem("wl1_loaded")
        a_loaded = [sem(f"a_loaded{k}") for k in range(SLOTS)]
        zeroed = sem("zeroed")
        consts = sem("consts")
        staged = sem("staged")
        stage_dve = sem("stage_dve")
        stage_act = sem("stage_act")
        bias_staged = sem("bias_staged")
        bias_ready = sem("bias_ready")
        turned = [sem("turned_l0"), sem("turned_l1")]
        squared_pool = sem("squared_pool")
        squared_act = sem("squared_act")
        tanh_done = sem("tanh_done")
        masked = sem("masked")
        half_used = [sem("half_used_l0"), sem("half_used_l1")]
        signed = sem("signed")
        counted = sem("counted")
        acc_read = [sem("acc_read_l0"), sem("acc_read_l1")]
        z_ready = sem("z_ready")
        rows_ready = sem("rows_ready")
        y_ready = sem("y_ready")
        ln_step = sem("ln_step")
        normed = sem("normed")
        cols_ready = sem("cols_ready")
        x1_ready = sem("x1_ready")
        stored = [sem("stored0"), sem("stored1")]
        stats_step = sem("stats_step")
        stats_pe = sem("stats_pe")
        flag_ready = sem("flag_ready")
        g_tile_free = sem("g_tile_free")
        g_loaded = [sem("g_loaded_l0"), sem("g_loaded_l1")]
        g_squared = sem("g_squared")
        g_tanh = sem("g_tanh")
        g_select = sem("g_select")
        g_picked = sem("g_picked")
        g_turned = sem("g_turned")
        g_split = sem("g_split")
        g_product = sem("g_product")
        g_added = sem("g_added")
        g_y_step = sem("g_y_step")
        g_row_turned = sem("g_row_turned")
        g_x1_kept = sem("g_x1_kept")
        g_w_picked = sem("g_w_picked")
        g_w_product = sem("g_w_product")
        g_w_kept = sem("g_w_kept")
        g_x1_picked = sem("g_x1_picked")
        g_x1_turned = sem("g_x1_turned")
        g_stored = sem("g_stored")

        def chunks(eng, body):
            body((0, 0, 0), None)
            with eng.Fori(0, (CHUNKS - 2) // 2) as pair:
                body((pair * 2 + 1, pair, 1), (pair * 2, pair, 0))
                body((pair * 2 + 2, pair + 1, 0), (pair * 2 + 1, pair, 1))
            body(LAST, (CHUNKS - 2, CHUNKS // 2 - 1, 0))

        def is_first(c):
            return isinstance(c, int) and c == 0

        GROUPS = CHUNKS
        EVEN_FIRST = [*range(0, GROUPS, 2), *range(1, GROUPS, 2)]
        turns, hids = ([(kind, g) for g in EVEN_FIRST] for kind in ("turn", "hid"))
        rhss = [("rhs", g) for g in range(GROUPS)]
        USES = turns[:3]
        for k in range(4):
            USES += [hids[k]] + turns[k + 3:k + 4]
        USES += turns[7:]
        for k in range(4):
            USES += [rhss[k], hids[k + 4]]
        USES += rhss[4:]
        by_dve = [k == "turn" or (k == "rhs" and g >= GROUPS // 2) for k, g in USES]

        def count_of(kind, g):
            n = USES.index((kind, g))
            return sum(by_dve[:n + 1]) if by_dve[n] else n + 1 - sum(by_dve[:n + 1])

        def emptied(eng, n, run):
            if by_dve[n]:
                eng.wait_ge(stage_dve, DVE_EMPTIED[run] + count_of(*USES[n]))
            else:
                eng.wait_ge(stage_act, ACT_EMPTIED[run] + count_of(*USES[n]))

        def g_tiles(eng, body):
            with eng.Fori(0, QUARTERS) as q:
                with eng.Fori(0, TPQ) as s:
                    body(q * TPQ + s, q, s)

        def when_failed(eng):
            eng.wait_ge(flag_ready, 1)
            failed = eng.value_load(flag[0:1, 0:1], min_val=0, max_val=1)
            return eng.If(failed > 0)

        N_DVE0, N_ACT0 = sum(by_dve), len(USES) - sum(by_dve)
        PQ = BLOCKS // TILES
        STAGED = (0, len(USES) + PQ)
        DVE_EMPTIED = (0, N_DVE0 + PQ)
        ACT_EMPTIED = (0, N_ACT0 + 2 * PQ)
        TPQ = ALL_TILES // QUARTERS
        ROUNDS = TOP // MAX8
        REST = TOP - ROUNDS * MAX8
        SELECT_STEPS = 2 * ROUNDS + 5

        block = ctx.enter_context(nc.Block())

        @block.gpsimd
        def _(pool):
            nc.gpsimd.memset(ident[:], 0.0).then_inc(zeroed, 1)
            nc.gpsimd.memset(ones[:], 1.0).then_inc(consts, 1)
            pool.wait_ge(zeroed, 1)
            nc.gpsimd.affine_select(out=ident[:], in_=ident[:], compare_op=ALU.not_equal, fill=1.0, base=0,
                                    pattern=[[-1, P]], channel_multiplier=1).then_inc(consts, 1)

            def layer0(chunk, before):
                for h in range(HPC):
                    part = a_cols[:, h % HSLOTS, 0:SQ_POOL, :]
                    pool.wait_ge(turned[0], chunk[0] * HPC + h + 1)
                    nc.gpsimd.tensor_tensor(part, part, part, ALU.mult).then_inc(squared_pool, 1)

            chunks(pool, layer0)

        @block.sync
        def _(sp):
            def load_x():
                for g in EVEN_FIRST:
                    sp.dma_start(xr[:, g * TILES:(g + 1) * TILES, :],
                                 x[g * CH:(g + 1) * CH, :].rearrange("(t p) f -> p t f", p=P))\
                        .then_inc(x_loaded[g], 16)

            load_x()

            def load_chunk(layer, c, first):
                fill = c + layer * CHUNKS
                for s in range(PIECES):
                    if layer == 0 and not first:
                        sp.wait_ge(turned[0], HPC * (c - 1) + HALVES * (s + 1))
                    if layer == 1 and first:
                        sp.wait_ge(turned[0], HPC * (CHUNKS - 1) + HALVES * (s + 1))
                    if layer == 1 and not first:
                        sp.wait_ge(counted, PIECES * (c - 1) + s + 1)
                    for q in range(QUARTERS):
                        src = adj[bass.ds(c * CH, CH), q * QUARTER + s * PCOLS:q * QUARTER + (s + 1) * PCOLS]
                        sp.dma_start(a_rows[SQ * q:SQ * (q + 1), s, :, :],
                                     src.rearrange("(r i) k -> i r k", i=SQ)).then_inc(a_loaded[s], 16)

            for layer in range(2):
                load_chunk(layer, 0, True)
                with sp.Fori(1, CHUNKS) as c:
                    load_chunk(layer, c, False)
            for k in range(2):
                sp.wait_ge(stored[k], 16 * CHUNKS // 2)

            with when_failed(sp):
                load_x()

                def g_load0(t, q, s):
                    sp.wait_ge(g_tile_free, t + 1)
                    sp.dma_start(g_in, adj[bass.ds(t * P, P), :]).then_inc(g_loaded[0], 16)
                    sp.dma_start(g_x, x[bass.ds(t * P, P), :]).then_inc(g_loaded[0], 16)

                def g_load1(t, q, s):
                    sp.wait_ge(g_tile_free, t + ALL_TILES + 1)
                    sp.dma_start(g_in, adj[bass.ds(t * P, P), :]).then_inc(g_loaded[1], 16)
                    sp.wait_ge(normed, t + 2 * CHUNKS + ALL_TILES + 1)
                    sp.dma_start(out[bass.ds(t * P, P), :], g_out).then_inc(g_stored, 16)

                g_tiles(sp, g_load0)
                g_tiles(sp, g_load1)
                sp.wait_ge(g_stored, 16 * ALL_TILES)

        @block.scalar
        def _(act):
            act.dma_start(w_pg[:, 0, :], w_proj).then_inc(small_loaded, 16)
            act.dma_start(w_pg[:, 1, :], w_gcn).then_inc(small_loaded, 16)
            for k, b in enumerate((b_proj, b_gcn)):
                act.dma_start(b_col[:, k:k + 1], b.rearrange("(p a) -> p a", a=1)).then_inc(small_loaded, 16)
            act.wait_ge(small_loaded, 64)

            def before_layer0(run):
                for n, (kind, g) in enumerate(USES):
                    if by_dve[n]:
                        continue
                    act.wait_ge(staged, STAGED[run] + n + 1)
                    if kind == "hid":
                        nc.scalar.activation(nodes(h_t, g // 2, g % 2), sets(stage[n % 4]), ACT.Tanh,
                                             bias=b_col[:, 0:1]).then_inc(stage_act, 1)
                    else:
                        nc.scalar.copy(rhs[:, g * TILES:(g + 1) * TILES, :],
                                       stage[n % 4][:].rearrange("p (b f) -> p b f", f=F)).then_inc(stage_act, 1)

            before_layer0(0)
            for k, b in enumerate((node_b, edge_b, b_gcn)):
                act.dma_start(b_row[:, k, :], b.rearrange("(a f) -> a f", a=1)).then_inc(wl1_loaded, 16)
            act.dma_start(w_pne[:, 0:2, :], node_w.rearrange("(s p) f -> p s f", p=P)).then_inc(wl1_loaded, 16)
            act.dma_start(w_pne[:, 2, :], edge_w).then_inc(wl1_loaded, 16)
            with nc.allow_non_contiguous_dma(reason="the diagonal"):
                act.dma_start(diag[:], bass.AP(adj.tensor, 0, [[N + 1, P], [P * (N + 1), ALL_TILES]]))\
                    .then_inc(wl1_loaded, 16)

            def x1_back(chunk):
                c, q, parity = chunk
                act.wait_ge(cols_ready, c + 1)
                nc.scalar.copy(nodes(feat_t[:], q, parity), sets(to_cols)).then_inc(x1_ready, 1)

            def relu_out(chunk):
                c, q, parity = chunk
                act.wait_ge(half_used[0], HPC * (c + 1))
                nc.scalar.activation(z_t[:], acc[parity][:], ACT.Relu, bias=b_col[:, 1:2])\
                    .then_inc(acc_read[0], 1)

            def layer0(chunk, before):
                c = chunk[0]
                for h in range(HPC):
                    if h == 3 and before:
                        relu_out(before)
                    n = c * HPC + h
                    hs = h % HSLOTS
                    act.wait_ge(turned[0], n + 1)
                    nc.scalar.activation(a_cols[:, hs, SQ_POOL:, :], a_cols[:, hs, SQ_POOL:, :], ACT.Square)\
                        .then_inc(squared_act, 1)
                    act.wait_ge(squared_act, n + 1)
                    act.wait_ge(squared_pool, n + 1)
                    nc.scalar.activation(a_cols[:, hs, :, :], a_cols[:, hs, :, :], ACT.Tanh)\
                        .then_inc(tanh_done, 1)
                if before:
                    x1_back(before)

            chunks(act, layer0)
            relu_out(LAST)
            for g in range(PQ):
                if g == PQ // 2:
                    x1_back(LAST)
                act.wait_ge(staged, len(USES) + g + 1)
                nc.scalar.copy(pos_hi[:, g * TILES:(g + 1) * TILES, :],
                               stage[g % 2][:].rearrange("p (b f) -> p b f", f=F)).then_inc(stage_act, 1)
                nc.scalar.copy(rhs[:, g * TILES:(g + 1) * TILES, :],
                               stage[2 + g % 2][:].rearrange("p (b f) -> p b f", f=F)).then_inc(stage_act, 1)

            def layer1(chunk, before):
                c = chunk[0]
                for s in range(PIECES):
                    piece = a_rows[:, s, :, :]
                    col = c * PIECES + s
                    act.wait_ge(turned[1], c * HPC + HALVES * (s + 1))
                    nc.scalar.activation(piece, piece, ACT.Sign, accum_out=signs[:, bass.ds(col, 1)])\
                        .then_inc(signed, 1)
                    act.wait_ge(signed, col + 1)
                    nc.scalar.activation(piece, piece, ACT.Relu, scale=-1.0,
                                         accum_out=negs[:, bass.ds(col, 1)]).then_inc(counted, 1)
                    if s == PIECES - 1 and before:
                        store(before)

            def store(chunk):
                c, q, parity = chunk
                act.wait_ge(normed, CHUNKS + c + 1)
                act.dma_start(out[bass.ds(c * CH, CH), :].rearrange("(t p) f -> p t f", p=P),
                              n_rows[:, parity, :, :]).then_inc(stored[parity], 16)

            chunks(act, layer1)
            store(LAST)

            with when_failed(act):
                before_layer0(1)

                def g_layer0(t, q, s):
                    act.wait_ge(g_squared, t + 1)
                    nc.scalar.activation(g_kept, g_work, ACT.Tanh).then_inc(g_tanh, 1)

                g_tiles(act, g_layer0)

        @block.vector
        def _(dve):
            EARLY = 2

            def turn(layer, c, h):
                s, hs = h // HALVES, h % HSLOTS
                n = c * HPC + h
                if h % HALVES == 0:
                    dve.wait_ge(a_loaded[s], 16 * QUARTERS * (c + layer * CHUNKS + 1))
                if h >= HSLOTS or not is_first(c):
                    dve.wait_ge(half_used[layer], n + 1 - HSLOTS)
                elif layer == 1:
                    dve.wait_ge(half_used[0], HPC * CHUNKS + n + 1 - HSLOTS)
                nc.vector.transpose(half_out(hs), half_in(s, h % HALVES)).then_inc(turned[layer], 1)
                return n, hs

            def before_layer0(run):
                for n, (kind, g) in enumerate(USES):
                    if not by_dve[n]:
                        continue
                    if kind == "rhs" and g == GROUPS // 2 and run == 0:
                        for h in range(EARLY):
                            turn(0, 0, h)
                    dve.wait_ge(staged, STAGED[run] + n + 1)
                    if kind == "turn":
                        nc.vector.tensor_copy(nodes(feat_t[:], g // 2, g % 2), sets(stage[n % 4]))\
                            .then_inc(stage_dve, 1)
                    else:
                        nc.vector.tensor_copy(rhs[:, g * TILES:(g + 1) * TILES, :],
                                              stage[n % 4][:].rearrange("p (b f) -> p b f", f=F))\
                            .then_inc(stage_dve, 1)

            before_layer0(0)

            def norm(base, src, dst, tiles):
                def step(k, ins):
                    ins.then_inc(ln_step, 1)
                    dve.wait_ge(ln_step, base + k)

                for k in range(tiles):
                    ins = nc.vector.bn_stats(bn[:, k, :], src(k))
                step(1, ins)
                v, y, t, m = var[:, 0:tiles], root[:, 0:tiles], tmp[:, 0:tiles], mean[:, 0:tiles]
                even, odd = bn[:, 0:tiles, 0:3], bn[:, 0:tiles, 3:6]
                nc.vector.tensor_tensor(t, even[:, :, 1], odd[:, :, 1], ALU.subtract)
                nc.vector.tensor_tensor(m, even[:, :, 1], odd[:, :, 1], ALU.add)
                step(2, nc.vector.tensor_tensor(v, even[:, :, 2], odd[:, :, 2], ALU.add))
                nc.vector.tensor_scalar(m, m, 0.5, None, ALU.mult)
                step(3, nc.vector.scalar_tensor_tensor(out=t, in0=t, scalar=0.25, in1=t, op0=ALU.mult, op1=ALU.mult))
                step(4, nc.vector.scalar_tensor_tensor(out=v, in0=v, scalar=1.0 / F, in1=t, op0=ALU.mult, op1=ALU.add))
                step(5, nc.vector.tensor_scalar(v, v, EPS, None, ALU.add))
                step(6, nc.vector.tensor_scalar(t.bitcast(i32), v.bitcast(i32), 1, None, ALU.logical_shift_right))
                step(7, nc.vector.tensor_scalar(y.bitcast(i32), t.bitcast(i32), -1.0, float(RSQRT_SEED),
                                                ALU.mult, ALU.add))
                for n in range(NEWTON):
                    k = 8 + 3 * n
                    step(k, nc.vector.scalar_tensor_tensor(out=t, in0=y, scalar=-0.5, in1=y, op0=ALU.mult, op1=ALU.mult))
                    step(k + 1, nc.vector.tensor_tensor(t, t, v, ALU.mult))
                    step(k + 2, nc.vector.scalar_tensor_tensor(out=y, in0=t, scalar=1.5, in1=y, op0=ALU.add, op1=ALU.mult))
                for k in range(tiles):
                    ins = nc.vector.tensor_scalar(dst(k), src(k), mean[:, k:k + 1], root[:, k:k + 1],
                                                  ALU.subtract, ALU.mult)
                return ins

            def residual0(chunk):
                c, q, parity = chunk
                dve.wait_ge(acc_read[0], c + 1)
                nc.vector.tensor_tensor(sets(z_t), sets(z_t), nodes(feat_t[:], q, parity), ALU.add)\
                    .then_inc(z_ready, 1)

            def norm0(chunk):
                c, q, parity = chunk
                dve.wait_ge(rows_ready, c + 1)
                norm(LN_STEPS * c, lambda k: to_rows[:, k, :], lambda k: n_rows[:, parity, k, :], TILES)\
                    .then_inc(normed, 1)

            def layer0(chunk, before):
                for h in range(0 if before else EARLY, HPC):
                    turn(0, chunk[0], h)
                    if h == 3 and before:
                        residual0(before)
                    if h == 5 and before:
                        norm0(before)

            chunks(dve, layer0)
            dve.wait_ge(bias_staged, 1)
            nc.vector.tensor_copy(bias_bc[:], stage[0][:, 0:2 * F].rearrange("p (k f) -> p k f", f=F))\
                .then_inc(bias_ready, 1)

            def low_part(g):
                dve.wait_ge(stage_act, N_ACT0 + 2 * g + 1)
                nc.vector.tensor_tensor(pos_lo[:, g * TILES:(g + 1) * TILES, :],
                                        stage[g % 2][:].rearrange("p (b f) -> p b f", f=F),
                                        pos_hi[:, g * TILES:(g + 1) * TILES, :].bitcast(f32),
                                        ALU.subtract).then_inc(stage_dve, 1)

            def before_layer1(h):
                if h == 0:
                    residual0(LAST)
                    low_part(0)
                    low_part(1)
                    norm0(LAST)
                    low_part(2)
                    low_part(3)
                elif h + 3 < PQ:
                    low_part(h + 3)

            def residual1(chunk):
                c, q, parity = chunk
                dve.wait_ge(half_used[1], HPC * (c + 1))
                nc.vector.tensor_tensor(sets(z_t), sets(acc[parity]), nodes(feat_t[:], q, parity), ALU.add)\
                    .then_inc(acc_read[1], 1)

            def norm1(chunk):
                c, q, parity = chunk
                dve.wait_ge(rows_ready, CHUNKS + c + 1)
                for k in range(TILES):
                    ins = nc.vector.scalar_tensor_tensor(out=y_rows[:, k, :], in0=bias_bc[:, 0, :],
                                                         scalar=diag[:, bass.ds(c * TILES + k, 1)],
                                                         in1=to_rows[:, k, :], op0=ALU.mult, op1=ALU.add)
                ins.then_inc(y_ready, 1)
                dve.wait_ge(y_ready, c + 1)
                if not isinstance(c, int) or c > 1:
                    dve.wait_ge(stored[parity], q * 16)
                norm(LN_STEPS * (CHUNKS + c), lambda k: y_rows[:, k, :], lambda k: n_rows[:, parity, k, :], TILES)\
                    .then_inc(normed, 1)

            def layer1(chunk, before):
                for h in range(HPC):
                    if not before:
                        before_layer1(h)
                    n, hs = turn(1, chunk[0], h)
                    dve.wait_ge(turned[1], n + 1)
                    nc.vector.tensor_scalar(masks[:, hs, :, :], a_cols[:, hs, :, :], 0.0, None, ALU.is_gt)\
                        .then_inc(masked, 1)
                    if h == 3 and before:
                        residual1(before)
                    if h == 5 and before:
                        norm1(before)

            chunks(dve, layer1)

            dve.wait_ge(counted, CHUNKS * PIECES)
            nc.vector.memset(fails[:], 0.0)
            nc.vector.reduce_sum(chunk_signs[:], signs[:].rearrange("p (c s) -> p c s", s=PIECES),
                                 axis=mybir.AxisListType.X).then_inc(stats_step, 1)
            dve.wait_ge(stats_step, 1)
            nc.vector.reduce_sum(fails[:, 1:2], negs[:], axis=mybir.AxisListType.X).then_inc(stats_step, 1)
            dve.wait_ge(stats_pe, 1)
            nc.vector.tensor_scalar(over[0:SQ, :], stage[0][0:SQ, 0:CHUNKS], float(TOP), None, ALU.is_gt)\
                .then_inc(stats_step, 1)
            dve.wait_ge(stats_step, 3)
            nc.vector.reduce_sum(fails[0:SQ, 0:1], over[0:SQ, :], axis=mybir.AxisListType.X).then_inc(stats_step, 1)
            residual1(LAST)
            norm1(LAST)
            dve.wait_ge(stats_pe, 2)
            nc.vector.reduce_sum(over[0:1, 0:1], stage[1][0:1, 0:2], axis=mybir.AxisListType.X)\
                .then_inc(stats_step, 1)
            dve.wait_ge(stats_step, 5)
            nc.vector.tensor_scalar(flag[:], over[0:1, 0:1], 0.0, None, ALU.is_gt).then_inc(flag_ready, 1)

            with when_failed(dve):
                before_layer0(1)

                def held(signal, value):
                    dve.wait_ge(signal, value)
                    nc.vector.memset(held_at[:, 0:1], 0.0)

                nc.vector.memset(top8[:], 0.0).then_inc(g_tile_free, 1)

                def keep_largest(t):
                    base = t * SELECT_STEPS
                    dve.wait_ge(g_loaded[0], t * 32 + 32)
                    nc.vector.scalar_tensor_tensor(out=g_work, in0=g_in, scalar=0.0, in1=g_in, op0=ALU.max,
                                                   op1=ALU.mult).then_inc(g_squared, 1)
                    dve.wait_ge(g_tanh, t + 1)
                    nc.vector.tensor_copy(g_work, g_kept).then_inc(g_select, 1)
                    with dve.Fori(0, ROUNDS) as r:
                        held(g_select, base + r * 2 + 1)
                        nc.vector.max(top8[:], g_work).then_inc(g_select, 1)
                        held(g_select, base + r * 2 + 2)
                        nc.vector.match_replace(out=g_work, in_to_replace=top8[:], in_values=g_work,
                                                imm_value=0.0).then_inc(g_select, 1)
                    done = base + 2 * ROUNDS
                    held(g_select, done + 1)
                    nc.vector.max(top8[:], g_work).then_inc(g_select, 1)
                    held(g_select, done + 2)
                    nc.vector.memset(top8[:, REST:MAX8], 0.0).then_inc(g_select, 1)
                    held(g_select, done + 3)
                    nc.vector.match_replace(out=g_work, in_to_replace=top8[:], in_values=g_work,
                                            imm_value=0.0).then_inc(g_select, 1)
                    dve.wait_ge(g_select, done + 4)
                    nc.vector.tensor_tensor(g_kept, g_kept, g_work, ALU.subtract).then_inc(g_select, 1)
                    held(g_select, done + 5)

                def g_contract(layer, u):
                    rows = g_blk(g_kept if layer == 0 else g_in)
                    nc.vector.memset(g_sum, 0.0).then_inc(g_added, 1)
                    with dve.Fori(0, BLOCKS) as b:
                        n = u * BLOCKS + b
                        nc.vector.tensor_copy(g_pick.rearrange("p (q j) -> p q j", j=SQ), rows[:, b, :, :])\
                            .then_inc(g_picked, 1)
                        dve.wait_ge(g_turned, n + 1)
                        last = nc.vector.tensor_copy(g_cols, stage[0][:, 0:P])
                        if layer == 1:
                            nc.vector.tensor_scalar(g_gt, stage[0][:, 0:P], 0.0, None, ALU.is_gt)
                            last = nc.vector.tensor_scalar(g_lt, stage[0][:, 0:P], 0.0, None, ALU.is_lt)
                        last.then_inc(g_split, 1)
                        dve.wait_ge(g_product, n + 1)
                        dve.wait_ge(g_added, n + u + 1)
                        nc.vector.tensor_tensor(g_sum, g_sum, stage[1][:, 0:F], ALU.add).then_inc(g_added, 1)
                    dve.wait_ge(g_added, (u + 1) * (BLOCKS + 1))

                def g_norm(u):
                    norm((u + 2 * CHUNKS) * LN_STEPS, lambda k: g_y, lambda k: g_out, 1).then_inc(normed, 1)

                def g_layer0(t, q, s):
                    keep_largest(t)
                    g_contract(0, t)
                    nc.vector.tensor_tensor(g_y, g_sum, bias_bc[:, 1, :], ALU.add).then_inc(g_y_step, 1)
                    dve.wait_ge(g_y_step, t * 2 + 1)
                    nc.vector.scalar_tensor_tensor(out=g_y, in0=g_y, scalar=0.0, in1=g_x, op0=ALU.max,
                                                   op1=ALU.add).then_inc(g_y_step, 1)
                    dve.wait_ge(g_y_step, t * 2 + 2)
                    g_norm(t)
                    dve.wait_ge(g_row_turned, t + 1)
                    nc.vector.tensor_copy(g_nodes(q, s), to_cols[:, 0:P].rearrange("f (b j) -> f b j", j=SQ))\
                        .then_inc(g_x1_kept, 1)
                    held(g_x1_kept, t + 1)
                    nc.vector.memset(held_at[:, 1:2], 0.0).then_inc(g_tile_free, 1)

                g_tiles(dve, g_layer0)

                with dve.Fori(0, BLOCKS) as b:
                    nc.vector.tensor_copy(g_pick, feat_t[:, bass.ds(b * P, P)]).then_inc(g_w_picked, 1)
                    dve.wait_ge(g_w_product, b + 1)
                    for k, kept in enumerate((g_pos, g_neg, rhs)):
                        last = nc.vector.tensor_copy(kept[:, b, :], stage[0][:, k * F:(k + 1) * F])
                    last.then_inc(g_w_kept, 1)
                dve.wait_ge(g_w_kept, BLOCKS)

                def g_layer1(t, q, s):
                    dve.wait_ge(g_loaded[1], t * 16 + 16)
                    g_contract(1, t + ALL_TILES)
                    nc.vector.tensor_copy(g_pick.rearrange("f (b j) -> f b j", j=SQ), g_nodes(q, s))\
                        .then_inc(g_x1_picked, 1)
                    dve.wait_ge(g_x1_turned, t + 1)
                    nc.vector.tensor_tensor(g_y, g_sum, to_cols[:, 0:P], ALU.add).then_inc(g_y_step, 1)
                    dve.wait_ge(g_y_step, (t + ALL_TILES) * 2 + 1)
                    nc.vector.scalar_tensor_tensor(out=g_y, in0=bias_bc[:, 0, :], scalar=diag[:, bass.ds(t, 1)],
                                                   in1=g_y, op0=ALU.mult, op1=ALU.add).then_inc(g_y_step, 1)
                    dve.wait_ge(g_y_step, (t + ALL_TILES) * 2 + 2)
                    g_norm(t + ALL_TILES)
                    held(g_stored, t * 16 + 16)
                    nc.vector.memset(held_at[:, 1:2], 0.0).then_inc(g_tile_free, 1)

                g_tiles(dve, g_layer1)

        @block.tensor
        def _(pe):
            pe.wait_ge(consts, 2)
            def before_layer0(run):
                for n, (kind, g) in enumerate(USES):
                    if n >= 4:
                        emptied(pe, n - 4, run)
                    bank = stage[n % 4]
                    if kind == "turn":
                        pe.wait_ge(x_loaded[g], 16 * (run + 1))
                        for k in range(TILES):
                            last = nc.tensor.transpose(bank[:, k * P:(k + 1) * P], xr[:, g * TILES + k, :], ident[:])
                    elif kind == "hid":
                        pe.wait_ge(small_loaded, 64)
                        pe.wait_ge(stage_dve, DVE_EMPTIED[run] + count_of("turn", g))
                        last = nc.tensor.matmul(bank[:], w_pg[:, 0, :], nodes(feat_t[:], g // 2, g % 2),
                                                start=True, stop=True)
                    else:
                        if g in (0, GROUPS // 2):
                            pe.wait_ge(stage_act, ACT_EMPTIED[run] + count_of("hid", GROUPS - 2 if g == 0 else GROUPS - 1))
                        for k in range(TILES):
                            last = nc.tensor.matmul(bank[:, k * P:(k + 1) * P], blk(h_t, g * TILES + k),
                                                    w_pg[:, 1, :], start=True, stop=True)
                    last.then_inc(staged, 1)

            before_layer0(0)
            def turn_to_rows(layer, c):
                if layer == 0:
                    pe.wait_ge(z_ready, c + 1)
                else:
                    pe.wait_ge(acc_read[1], c + 1)
                if layer == 1 or not isinstance(c, int) or c > 0:
                    pe.wait_ge(normed, layer * CHUNKS + c)
                for k in range(TILES):
                    last = nc.tensor.transpose(to_rows[:, k, :], z_t[:, k * P:(k + 1) * P], ident[:])
                last.then_inc(rows_ready, 1)

            def turn_x1_back(chunk):
                c, q, parity = chunk
                pe.wait_ge(normed, c + 1)
                if not isinstance(c, int) or c > 0:
                    pe.wait_ge(x1_ready, c)
                for k in range(TILES):
                    last = nc.tensor.transpose(to_cols[:, k * P:(k + 1) * P], n_rows[:, parity, k, :], ident[:])
                last.then_inc(cols_ready, 1)

            def layer0(chunk, before):
                c, q, parity = chunk
                if not isinstance(c, int) or c > 1:
                    pe.wait_ge(acc_read[0], c - 1)
                for h in range(HPC):
                    n = c * HPC + h
                    if not before:
                        if h < GROUPS // 2:
                            pe.wait_ge(stage_act, count_of("rhs", h))
                        else:
                            pe.wait_ge(stage_dve, count_of("rhs", h))
                    pe.wait_ge(tanh_done, n + 1)
                    for k in range(HB):
                        b = h * HB + k
                        last = nc.tensor.matmul(acc[parity][:], rhs[:, b, :], a_cols[:, h % HSLOTS, k, :],
                                                start=(b == 0), stop=(b == BLOCKS - 1))
                    last.then_inc(half_used[0], 1)
                    if h == 1 and before:
                        turn_to_rows(0, before[0])
                    if h == 4 and before:
                        turn_x1_back(before)

            chunks(pe, layer0)
            pe.wait_ge(wl1_loaded, 96)
            nc.tensor.matmul(stage[0][:, 0:F], ones[0:1, :], b_row[:, 0, :], start=True, stop=False)
            nc.tensor.matmul(stage[0][:, 0:F], ones[0:1, :], b_row[:, 1, :], start=False, stop=True)
            nc.tensor.matmul(stage[0][:, F:2 * F], ones[0:1, :], b_row[:, 2, :], start=True, stop=True)\
                .then_inc(bias_staged, 1)

            def operands(g):
                if g == 0:
                    pe.wait_ge(x1_ready, CHUNKS - 1)
                    pe.wait_ge(bias_ready, 1)
                if g == PQ // 2:
                    pe.wait_ge(x1_ready, CHUNKS)
                if g >= 2:
                    pe.wait_ge(stage_act, N_ACT0 + 2 * (g - 1))
                    pe.wait_ge(stage_dve, N_DVE0 + g - 1)
                for k in range(TILES):
                    for part, w in ((0, 0), (2, 2)):
                        last = nc.tensor.matmul(stage[part + g % 2][:, k * P:(k + 1) * P],
                                                blk(feat_t[:], g * TILES + k), w_pne[:, w, :],
                                                start=True, stop=True)
                last.then_inc(staged, 1)

            def before_layer1(h):
                if h == 0:
                    operands(0)
                    operands(1)
                    turn_to_rows(0, CHUNKS - 1)
                    operands(2)
                    operands(3)
                    turn_x1_back(LAST)
                    operands(4)
                elif h + 4 < PQ:
                    operands(h + 4)
                pe.wait_ge(stage_act, N_ACT0 + 2 * (h + 1))
                pe.wait_ge(stage_dve, N_DVE0 + h + 1)

            def layer1(chunk, before):
                c, q, parity = chunk
                if not isinstance(c, int) or c > 1:
                    pe.wait_ge(acc_read[1], c - 1)
                for h in range(HPC):
                    n = c * HPC + h
                    if not before:
                        before_layer1(h)
                    if chunk is LAST and h == HPC - 1:
                        sum_signs()
                    pe.wait_ge(masked, n + 1)
                    for k in range(HB):
                        b = h * HB + k
                        cols, mask = a_cols[:, h % HSLOTS, k, :], masks[:, h % HSLOTS, k, :]
                        nc.tensor.matmul(acc[parity][:], rhs[:, b, :], cols, start=(b == 0), stop=False)
                        nc.tensor.matmul(acc[parity][:], pos_hi[:, b, :], mask, start=False, stop=False)
                        last = nc.tensor.matmul(acc[parity][:], pos_lo[:, b, :], mask, start=False,
                                                stop=(b == BLOCKS - 1))
                    last.then_inc(half_used[1], 1)
                    if h == 1 and before:
                        turn_to_rows(1, before[0])

            def sum_signs():
                pe.wait_ge(stats_step, 1)
                for q in range(QUARTERS):
                    last = nc.tensor.matmul(stage[0][0:SQ, 0:CHUNKS], ident[:, q * SQ:(q + 1) * SQ], chunk_signs[:],
                                            start=(q == 0), stop=(q == QUARTERS - 1))
                last.then_inc(stats_pe, 1)

            chunks(pe, layer1)
            turn_to_rows(1, CHUNKS - 1)
            pe.wait_ge(stats_step, 4)
            nc.tensor.matmul(stage[1][0:1, 0:2], ones[:, 0:1], fails[:], start=True, stop=True).then_inc(stats_pe, 1)

            with when_failed(pe):
                before_layer0(1)
                pe.wait_ge(stage_dve, DVE_EMPTIED[1] + N_DVE0)
                pe.wait_ge(stage_act, ACT_EMPTIED[1] + N_ACT0)

                def g_contract(layer, u):
                    with pe.Fori(0, BLOCKS) as b:
                        n = u * BLOCKS + b
                        pe.wait_ge(g_picked, n + 1)
                        nc.tensor.transpose(stage[0][:, 0:P], g_pick, ident[:]).then_inc(g_turned, 1)
                        pe.wait_ge(g_split, n + 1)
                        parts = [(g_cols, rhs)] + [(g_gt, g_pos), (g_lt, g_neg)] * layer
                        for k, (cols, operand) in enumerate(parts):
                            last = nc.tensor.matmul(stage[1][:, 0:F], cols, operand[:, b, :], start=(k == 0),
                                                    stop=(k == len(parts) - 1))
                        last.then_inc(g_product, 1)

                def g_layer0(t, q, s):
                    g_contract(0, t)
                    pe.wait_ge(normed, t + 2 * CHUNKS + 1)
                    nc.tensor.transpose(to_cols[:, 0:P], g_out, ident[:]).then_inc(g_row_turned, 1)

                g_tiles(pe, g_layer0)
                with pe.Fori(0, BLOCKS) as b:
                    pe.wait_ge(g_w_picked, b + 1)
                    nc.tensor.matmul(stage[0][:, 0:3 * F], g_pick, w_pne[:].rearrange("p k f -> p (k f)"),
                                     start=True, stop=True).then_inc(g_w_product, 1)

                def g_layer1(t, q, s):
                    g_contract(1, t + ALL_TILES)
                    pe.wait_ge(g_x1_picked, t + 1)
                    nc.tensor.transpose(to_cols[:, 0:P], g_pick, ident[:]).then_inc(g_x1_turned, 1)

                g_tiles(pe, g_layer1)


_INS = ['x', 'adj', 'L0_gnn_W_proj', 'L0_gnn_b_proj', 'L0_gnn_W_gcn', 'L0_gnn_b_gcn', 'L1_gnn_node_weight',
        'L1_gnn_node_bias', 'L1_gnn_edge_weight', 'L1_gnn_edge_bias']


def kernel(**inputs):
    import concourse.bacc as _bacc
    from concourse.bass_utils import run_bass_kernel_spmd as _run

    nc = _bacc.Bacc("TRN2", target_bir_lowering=False, num_devices=1)
    arrays, args = {}, []
    for name in _INS:
        a = np.ascontiguousarray(inputs[name])
        arrays[f"in_{name}_dram"] = a
        args.append(nc.dram_tensor(f"in_{name}_dram", a.shape, mybir.dt.from_np(a.dtype), kind="ExternalInput").ap())
    shape = inputs['x'].shape
    args.append(nc.dram_tensor("out_dram", shape, mybir.dt.float32, kind="ExternalOutput").ap())
    build(nc, *args)
    r = _run(nc, [arrays], core_ids=[0])
    return r.results[0]["out_dram"]
```

```python
import concourse.bass as bass
from concourse import mybir
from concourse.alu_op_type import AluOpType as ALU
from contextlib import ExitStack
import numpy as np


P = 128
SQ = 32
F = 128
TOP = 350
EPS = 1e-5
MAX8 = 8
RSQRT_SEED = 0x5F3759DF
NEWTON = 3
LN_STEPS = 5 + 3 * NEWTON


def build(nc, x, adj, w_proj, b_proj, w_gcn, b_gcn, node_w, node_b, edge_w, edge_b, out):
    f32, f32r, i32 = mybir.dt.float32, mybir.dt.float32r, mybir.dt.int32
    ACT = mybir.ActivationFunctionType

    N = adj.shape[0]
    QUARTERS = P // SQ
    QUARTER = N // QUARTERS
    BLOCKS = N // P
    CH = 512
    CHUNKS = N // CH
    ROWSETS = CH // SQ
    TILES = CH // P
    ALL_TILES = N // P
    PIECES = 4
    PCOLS = QUARTER // PIECES
    HALVES = 2
    HB = PCOLS // HALVES // SQ
    SLOTS = 4
    HSLOTS = 4
    HPC = PIECES * HALVES
    LAST = (CHUNKS - 1, CHUNKS // 2 - 1, 1)
    SQ_POOL = HB // 2
    PARTS = [(0, TILES // 2), (TILES // 2, TILES // 2)]
    TOGETHER = 3
    NORMS = 2 * CHUNKS + 1

    ctx = ExitStack()
    with ctx:
        def sb(name, shape, dt=f32):
            return ctx.enter_context(nc.sbuf_tensor(name, shape, dt))

        def pb(name, shape):
            return ctx.enter_context(nc.psum_tensor(name, shape, f32))

        def sem(name):
            return ctx.enter_context(nc.semaphore(name))

        shared_at = -(-nc.sbuf_base // SQ) * SQ
        sb("shared", [P, HSLOTS * HB * CH])
        masks = nc.alloc_sbuf_tensor_at("masks", [P, HSLOTS, HB, CH], f32r, offset=shared_at)
        early = nc.alloc_sbuf_tensor_at("early", [P, 2, N], f32, offset=shared_at)
        a_rows = sb("a_rows", [P, SLOTS, ROWSETS, PCOLS])
        a_cols = sb("a_cols", [P, HSLOTS, HB, CH])
        feat_t = sb("feat_t", [P, N])
        rhs = sb("rhs", [P, BLOCKS, F])
        pos_hi = sb("pos_hi", [P, BLOCKS, F], f32r)
        pos_lo = sb("pos_lo", [P, BLOCKS, F], f32r)
        z_t = sb("z_t", [P, CH])
        y_rows = sb("y_rows", [P, TILES, F])
        n_rows = sb("n_rows", [P, 2, TILES, F])
        w_pg = sb("w_pg", [P, 2, F])
        w_pne = sb("w_pne", [P, 3, F])
        b_col = sb("b_col", [P, 2])
        b_row = sb("b_row", [1, 3, F])
        bias_bc = sb("bias_bc", [P, 2, F])
        diag = sb("diag", [P, ALL_TILES])
        ident = sb("ident", [P, P])
        ones = sb("ones", [P, P])
        bn = sb("bn", [P, TILES, 6])
        mean = sb("mean", [P, TILES])
        var = sb("var", [P, TILES])
        root = sb("root", [P, TILES])
        tmp = sb("tmp", [P, TILES])
        signs = sb("signs", [P, CHUNKS * PIECES])
        negs = sb("negs", [P, CHUNKS * PIECES])
        chunk_signs = sb("chunk_signs", [P, CHUNKS])
        over = sb("over", [P, CHUNKS])
        fails = sb("fails", [P, 2])
        flag = sb("flag", [1, 1], i32)
        top8 = sb("top8", [P, MAX8])
        held_at = sb("held_at", [P, 2])

        acc = [pb(f"acc{k}", [P, CH]) for k in range(2)]
        to_rows = pb("to_rows", [P, TILES, F])
        to_cols = pb("to_cols", [P, CH])
        stage = [pb(f"stage{k}", [P, CH]) for k in range(4)]
        last_acc = [acc[LAST[2]], stage[2]]
        last_rows = [to_rows[:, 0:PARTS[0][1], :],
                     to_cols[:, 0:PARTS[1][1] * F].rearrange("p (t f) -> p t f", f=F)]

        def half_in(slot, h):
            w = PCOLS // HALVES
            return a_rows[:, slot, :, h * w:(h + 1) * w].rearrange("p r (b j) -> p r b j", j=SQ)

        def half_out(hs):
            return a_cols[:, hs, :, :].rearrange("p b (r i) -> p r b i", i=SQ)

        def blk(t, b):
            return t[:, b * P:(b + 1) * P]

        def nodes(t, q, parity):
            t = t.rearrange("f (b q j) -> f q b j", q=QUARTERS, j=SQ)
            return t[:, q, parity * ROWSETS:(parity + 1) * ROWSETS, :]

        def sets(t):
            return t[:].rearrange("f (b j) -> f b j", j=SQ)

        xr = early[:, 1, :].rearrange("p (t f) -> p t f", f=F)
        h_t = early[:, 0, :]

        def row(k):
            return a_rows[:, k, :, :].rearrange("p r c -> p (r c)")

        g_in, g_work, g_kept = row(0), row(1), row(2)
        g_small = row(3).rearrange("p (k f) -> p k f", f=F)
        g_pick, g_cols, g_gt, g_lt, g_sum, g_x, g_y = (g_small[:, k, :] for k in range(7))
        g_out = n_rows[:, 0, 0, :]
        g_pos = a_cols[:, 0:2, :, :].rearrange("p s b c -> p (s b c)").rearrange("p (b f) -> p b f", f=F)
        g_neg = a_cols[:, 2:4, :, :].rearrange("p s b c -> p (s b c)").rearrange("p (b f) -> p b f", f=F)

        def g_blk(t):
            return t.rearrange("p (q b j) -> p b q j", q=QUARTERS, j=SQ)

        def g_nodes(q, s):
            t = feat_t[:].rearrange("f (b q j) -> f q b j", q=QUARTERS, j=SQ)
            return t[:, q, bass.ds(s * QUARTERS, QUARTERS), :]

        x_loaded = [sem(f"x_loaded{g}") for g in range(CHUNKS)]
        small_loaded = sem("small_loaded")
        wl1_loaded = sem("wl1_loaded")
        a_loaded = [sem(f"a_loaded{k}") for k in range(SLOTS)]
        zeroed = sem("zeroed")
        consts = sem("consts")
        staged = sem("staged")
        stage_dve = sem("stage_dve")
        stage_act = sem("stage_act")
        bias_staged = sem("bias_staged")
        bias_ready = sem("bias_ready")
        turned = [sem("turned_l0"), sem("turned_l1")]
        squared_pool = sem("squared_pool")
        squared_act = sem("squared_act")
        tanh_done = sem("tanh_done")
        masked = sem("masked")
        half_used = [sem("half_used_l0"), sem("half_used_l1")]
        signed = sem("signed")
        counted = sem("counted")
        acc_read = [sem("acc_read_l0"), sem("acc_read_l1")]
        z_ready = sem("z_ready")
        rows_ready = sem("rows_ready")
        last_summed = sem("last_summed")
        y_ready = sem("y_ready")
        ln_step = sem("ln_step")
        normed = sem("normed")
        cols_ready = sem("cols_ready")
        x1_ready = sem("x1_ready")
        stored = [sem("stored0"), sem("stored1")]
        stats_step = sem("stats_step")
        stats_pe = sem("stats_pe")
        flag_ready = sem("flag_ready")
        g_tile_free = sem("g_tile_free")
        g_loaded = [sem("g_loaded_l0"), sem("g_loaded_l1")]
        g_squared = sem("g_squared")
        g_tanh = sem("g_tanh")
        g_select = sem("g_select")
        g_picked = sem("g_picked")
        g_turned = sem("g_turned")
        g_split = sem("g_split")
        g_product = sem("g_product")
        g_added = sem("g_added")
        g_y_step = sem("g_y_step")
        g_row_turned = sem("g_row_turned")
        g_x1_kept = sem("g_x1_kept")
        g_w_picked = sem("g_w_picked")
        g_w_product = sem("g_w_product")
        g_w_kept = sem("g_w_kept")
        g_x1_picked = sem("g_x1_picked")
        g_x1_turned = sem("g_x1_turned")
        g_stored = sem("g_stored")

        def chunks(eng, body):
            body((0, 0, 0), None)
            with eng.Fori(0, (CHUNKS - 2) // 2) as pair:
                body((pair * 2 + 1, pair, 1), (pair * 2, pair, 0))
                body((pair * 2 + 2, pair + 1, 0), (pair * 2 + 1, pair, 1))
            body(LAST, (CHUNKS - 2, CHUNKS // 2 - 1, 0))

        def rows_of(chunk):
            c, q, parity = chunk
            return c * -1 + (CHUNKS - 1), q * -1 + (QUARTERS - 1), 1 - parity

        def is_first(c):
            return isinstance(c, int) and c == 0

        GROUPS = CHUNKS
        EVEN_FIRST = [*range(0, GROUPS, 2), *range(1, GROUPS, 2)]
        turns, hids = ([(kind, g) for g in EVEN_FIRST] for kind in ("turn", "hid"))
        rhss = [("rhs", g) for g in range(GROUPS)]
        USES = turns[:3]
        for k in range(4):
            USES += [hids[k]] + turns[k + 3:k + 4]
        USES += turns[7:]
        for k in range(3):
            USES += [rhss[k], hids[k + 4]]
        USES += hids[7:] + rhss[3:]
        by_dve = [k == "turn" or (k == "rhs" and g >= GROUPS // 2) for k, g in USES]

        def count_of(kind, g):
            n = USES.index((kind, g))
            return sum(by_dve[:n + 1]) if by_dve[n] else n + 1 - sum(by_dve[:n + 1])

        def emptied(eng, n, run):
            if by_dve[n]:
                eng.wait_ge(stage_dve, DVE_EMPTIED[run] + count_of(*USES[n]))
            else:
                eng.wait_ge(stage_act, ACT_EMPTIED[run] + count_of(*USES[n]))

        def g_tiles(eng, body):
            with eng.Fori(0, QUARTERS) as q:
                with eng.Fori(0, TPQ) as s:
                    body(q * TPQ + s, q, s)

        def when_failed(eng):
            eng.wait_ge(flag_ready, 1)
            failed = eng.value_load(flag[0:1, 0:1], min_val=0, max_val=1)
            return eng.If(failed > 0)

        N_DVE0, N_ACT0 = sum(by_dve), len(USES) - sum(by_dve)
        PQ = BLOCKS // TILES
        STAGED = (0, len(USES) + PQ)
        DVE_EMPTIED = (0, N_DVE0 + PQ)
        ACT_EMPTIED = (0, N_ACT0 + 2 * PQ)
        TPQ = ALL_TILES // QUARTERS
        ROUNDS = TOP // MAX8
        REST = TOP - ROUNDS * MAX8
        SELECT_STEPS = 2 * ROUNDS + 5

        block = ctx.enter_context(nc.Block())

        @block.gpsimd
        def _(pool):
            nc.gpsimd.memset(ident[:], 0.0).then_inc(zeroed, 1)
            nc.gpsimd.memset(ones[:], 1.0).then_inc(consts, 1)
            pool.wait_ge(zeroed, 1)
            nc.gpsimd.affine_select(out=ident[:], in_=ident[:], compare_op=ALU.not_equal, fill=1.0, base=0,
                                    pattern=[[-1, P]], channel_multiplier=1).then_inc(consts, 1)

            def layer0(chunk, before):
                for h in range(HPC):
                    part = a_cols[:, h % HSLOTS, 0:SQ_POOL, :]
                    pool.wait_ge(turned[0], chunk[0] * HPC + h + 1)
                    nc.gpsimd.tensor_tensor(part, part, part, ALU.mult).then_inc(squared_pool, 1)

            chunks(pool, layer0)

        @block.sync
        def _(sp):
            def load_x():
                for g in EVEN_FIRST:
                    sp.dma_start(xr[:, g * TILES:(g + 1) * TILES, :],
                                 x[g * CH:(g + 1) * CH, :].rearrange("(t p) f -> p t f", p=P))\
                        .then_inc(x_loaded[g], 16)

            load_x()

            def load_chunk(layer, c):
                r = c * -1 + (CHUNKS - 1) if layer == 1 else c
                for s in range(PIECES):
                    if layer == 0 and not is_first(c):
                        sp.wait_ge(turned[0], HPC * (c - 1) + HALVES * (s + 1))
                    if layer == 1:
                        sp.wait_ge(counted, PIECES * (c - 1) + s + 1)
                    for q in range(QUARTERS):
                        src = adj[bass.ds(r * CH, CH), q * QUARTER + s * PCOLS:q * QUARTER + (s + 1) * PCOLS]
                        sp.dma_start(a_rows[SQ * q:SQ * (q + 1), s, :, :],
                                     src.rearrange("(r i) k -> i r k", i=SQ)).then_inc(a_loaded[s], 16)

            load_chunk(0, 0)
            for k, b in enumerate((node_b, edge_b, b_gcn)):
                sp.dma_start(b_row[:, k, :], b.rearrange("(a f) -> a f", a=1)).then_inc(wl1_loaded, 16)
            sp.dma_start(w_pne[:, 0:2, :], node_w.rearrange("(s p) f -> p s f", p=P)).then_inc(wl1_loaded, 16)
            sp.dma_start(w_pne[:, 2, :], edge_w).then_inc(wl1_loaded, 16)
            with nc.allow_non_contiguous_dma(reason="the diagonal"):
                sp.dma_start(diag[:], bass.AP(adj.tensor, 0, [[N + 1, P], [P * (N + 1), ALL_TILES]]))\
                    .then_inc(wl1_loaded, 16)
            for layer in range(2):
                with sp.Fori(1, CHUNKS) as c:
                    load_chunk(layer, c)
            sp.wait_ge(stored[0], 16 * (CHUNKS // 2))
            sp.wait_ge(stored[1], 16 * (CHUNKS // 2 + 1))

            with when_failed(sp):
                load_x()

                def g_load0(t, q, s):
                    sp.wait_ge(g_tile_free, t + 1)
                    sp.dma_start(g_in, adj[bass.ds(t * P, P), :]).then_inc(g_loaded[0], 16)
                    sp.dma_start(g_x, x[bass.ds(t * P, P), :]).then_inc(g_loaded[0], 16)

                def g_load1(t, q, s):
                    sp.wait_ge(g_tile_free, t + ALL_TILES + 1)
                    sp.dma_start(g_in, adj[bass.ds(t * P, P), :]).then_inc(g_loaded[1], 16)
                    sp.wait_ge(normed, t + NORMS + ALL_TILES + 1)
                    sp.dma_start(out[bass.ds(t * P, P), :], g_out).then_inc(g_stored, 16)

                g_tiles(sp, g_load0)
                g_tiles(sp, g_load1)
                sp.wait_ge(g_stored, 16 * ALL_TILES)

        @block.scalar
        def _(act):
            act.dma_start(w_pg[:, 0, :], w_proj).then_inc(small_loaded, 16)
            act.dma_start(w_pg[:, 1, :], w_gcn).then_inc(small_loaded, 16)
            for k, b in enumerate((b_proj, b_gcn)):
                act.dma_start(b_col[:, k:k + 1], b.rearrange("(p a) -> p a", a=1)).then_inc(small_loaded, 16)
            act.wait_ge(consts, 2)
            nc.scalar.activation(signs[:, 0:1], ones[:, 0:1], ACT.Tanh)
            act.wait_ge(small_loaded, 64)

            def before_layer0(run):
                for n, (kind, g) in enumerate(USES):
                    if by_dve[n]:
                        continue
                    act.wait_ge(staged, STAGED[run] + n + 1)
                    if kind == "hid":
                        nc.scalar.activation(nodes(h_t, g // 2, g % 2), sets(stage[n % 4]), ACT.Tanh,
                                             bias=b_col[:, 0:1]).then_inc(stage_act, 1)
                    else:
                        nc.scalar.copy(rhs[:, g * TILES:(g + 1) * TILES, :],
                                       stage[n % 4][:].rearrange("p (b f) -> p b f", f=F)).then_inc(stage_act, 1)

            before_layer0(0)
            def x1_back(chunk):
                c, q, parity = chunk
                act.wait_ge(cols_ready, c + 1)
                nc.scalar.copy(nodes(feat_t[:], q, parity), sets(to_cols)).then_inc(x1_ready, 1)

            def relu_out(chunk):
                c, q, parity = chunk
                act.wait_ge(half_used[0], HPC * (c + 1))
                nc.scalar.activation(z_t[:], acc[parity][:], ACT.Relu, bias=b_col[:, 1:2])\
                    .then_inc(acc_read[0], 1)

            def layer0(chunk, before):
                c = chunk[0]
                for h in range(HPC):
                    if h == 3 and before:
                        relu_out(before)
                    n = c * HPC + h
                    hs = h % HSLOTS
                    act.wait_ge(turned[0], n + 1)
                    nc.scalar.activation(a_cols[:, hs, SQ_POOL:, :], a_cols[:, hs, SQ_POOL:, :], ACT.Square)\
                        .then_inc(squared_act, 1)
                    act.wait_ge(squared_act, n + 1)
                    act.wait_ge(squared_pool, n + 1)
                    nc.scalar.activation(a_cols[:, hs, :, :], a_cols[:, hs, :, :], ACT.Tanh)\
                        .then_inc(tanh_done, 1)
                if before:
                    x1_back(before)

            chunks(act, layer0)
            relu_out(LAST)
            for g in range(PQ):
                if g == PQ // 2:
                    x1_back(LAST)
                act.wait_ge(staged, len(USES) + g + 1)
                nc.scalar.copy(pos_hi[:, g * TILES:(g + 1) * TILES, :],
                               stage[g % 2][:].rearrange("p (b f) -> p b f", f=F)).then_inc(stage_act, 1)
                nc.scalar.copy(rhs[:, g * TILES:(g + 1) * TILES, :],
                               stage[2 + g % 2][:].rearrange("p (b f) -> p b f", f=F)).then_inc(stage_act, 1)

            def layer1(chunk, before):
                c = chunk[0]
                for s in range(PIECES):
                    piece = a_rows[:, s, :, :]
                    col = c * PIECES + s
                    act.wait_ge(turned[1], c * HPC + HALVES * (s + 1))
                    nc.scalar.activation(piece, piece, ACT.Sign, accum_out=signs[:, bass.ds(col, 1)])\
                        .then_inc(signed, 1)
                    act.wait_ge(signed, col + 1)
                    nc.scalar.activation(piece, piece, ACT.Relu, scale=-1.0,
                                         accum_out=negs[:, bass.ds(col, 1)]).then_inc(counted, 1)
                    if s == PIECES - 1 and before:
                        store(before)

            def store(chunk):
                parity = chunk[2]
                for k, (at, tiles) in enumerate(PARTS if chunk is LAST else [(0, TILES)]):
                    act.wait_ge(normed, CHUNKS + chunk[0] + k + 1)
                    act.dma_start(out[bass.ds((rows_of(chunk)[0] * TILES + at) * P, tiles * P), :]
                                  .rearrange("(t p) f -> p t f", p=P),
                                  n_rows[:, parity, at:at + tiles, :]).then_inc(stored[parity], 16)

            chunks(act, layer1)
            store(LAST)

            with when_failed(act):
                before_layer0(1)

                def g_layer0(t, q, s):
                    act.wait_ge(g_squared, t + 1)
                    nc.scalar.activation(g_kept, g_work, ACT.Tanh).then_inc(g_tanh, 1)

                g_tiles(act, g_layer0)

        @block.vector
        def _(dve):
            EARLY = 3

            def turn(layer, c, h):
                s, hs = h // HALVES, h % HSLOTS
                n = c * HPC + h
                if h % HALVES == 0 and not (layer == 1 and is_first(c)):
                    dve.wait_ge(a_loaded[s], 16 * QUARTERS * (c + layer * (CHUNKS - 1) + 1))
                if h >= HSLOTS or not is_first(c):
                    dve.wait_ge(half_used[layer], n + 1 - HSLOTS)
                elif layer == 1:
                    dve.wait_ge(half_used[0], HPC * CHUNKS + n + 1 - HSLOTS)
                nc.vector.transpose(half_out(hs), half_in(s, h % HALVES)).then_inc(turned[layer], 1)
                return n, hs

            def before_layer0(run):
                for n, (kind, g) in enumerate(USES):
                    if not by_dve[n]:
                        continue
                    if kind == "rhs" and g == GROUPS // 2 and run == 0:
                        for h in range(EARLY):
                            turn(0, 0, h)
                    dve.wait_ge(staged, STAGED[run] + n + 1)
                    if kind == "turn":
                        nc.vector.tensor_copy(nodes(feat_t[:], g // 2, g % 2), sets(stage[n % 4]))\
                            .then_inc(stage_dve, 1)
                    else:
                        nc.vector.tensor_copy(rhs[:, g * TILES:(g + 1) * TILES, :],
                                              stage[n % 4][:].rearrange("p (b f) -> p b f", f=F))\
                            .then_inc(stage_dve, 1)

            before_layer0(0)

            def norm(base, src, dst, tiles):
                v, y, t, m = var[:, 0:tiles], root[:, 0:tiles], tmp[:, 0:tiles], mean[:, 0:tiles]
                even, odd = bn[:, 0:tiles, 0:3], bn[:, 0:tiles, 3:6]

                def step(k, ins):
                    ins.then_inc(ln_step, 1)
                    dve.wait_ge(ln_step, base + k)

                def variance():
                    for k in range(tiles):
                        ins = nc.vector.bn_stats(bn[:, k, :], src(k))
                    step(1, ins)
                    nc.vector.tensor_tensor(t, even[:, :, 1], odd[:, :, 1], ALU.subtract)
                    nc.vector.tensor_tensor(m, even[:, :, 1], odd[:, :, 1], ALU.add)
                    step(2, nc.vector.tensor_tensor(v, even[:, :, 2], odd[:, :, 2], ALU.add))
                    nc.vector.tensor_scalar(m, m, 0.5, None, ALU.mult)
                    nc.vector.tensor_scalar(v, v, 1.0 / F, EPS, ALU.mult, ALU.add)
                    step(3, nc.vector.scalar_tensor_tensor(out=t, in0=t, scalar=0.25, in1=t, op0=ALU.mult,
                                                           op1=ALU.mult))
                    step(4, nc.vector.tensor_tensor(v, v, t, ALU.add))
                    step(5, nc.vector.tensor_scalar(y.bitcast(i32), v.bitcast(i32), -0.5, float(RSQRT_SEED),
                                                    ALU.mult, ALU.add))

                def newton():
                    for n in range(NEWTON):
                        k = 6 + 3 * n
                        step(k, nc.vector.scalar_tensor_tensor(out=t, in0=y, scalar=-0.5, in1=y, op0=ALU.mult,
                                                               op1=ALU.mult))
                        step(k + 1, nc.vector.tensor_tensor(t, t, v, ALU.mult))
                        step(k + 2, nc.vector.scalar_tensor_tensor(out=y, in0=t, scalar=1.5, in1=y, op0=ALU.add,
                                                                   op1=ALU.mult))

                def scaled():
                    for k in range(tiles):
                        ins = nc.vector.tensor_scalar(dst(k), src(k), mean[:, k:k + 1], root[:, k:k + 1],
                                                      ALU.subtract, ALU.mult)
                    ins.then_inc(normed, 1)

                return variance, newton, scaled

            def residual0(chunk):
                c, q, parity = chunk
                dve.wait_ge(acc_read[0], c + 1)
                nc.vector.tensor_tensor(sets(z_t), sets(z_t), nodes(feat_t[:], q, parity), ALU.add)\
                    .then_inc(z_ready, 1)

            def norm0(chunk, part):
                c, q, parity = chunk
                if part == 0:
                    dve.wait_ge(rows_ready, c + 1)
                norm(LN_STEPS * c, lambda k: to_rows[:, k, :], lambda k: n_rows[:, parity, k, :], TILES)[part]()

            def layer0(chunk, before):
                for h in range(0 if before else EARLY, HPC):
                    turn(0, chunk[0], h)
                    if h == 3 and before:
                        residual0(before)
                    if h >= 5 and before:
                        norm0(before, h - 5)
                    if chunk is LAST and h == 4:
                        dve.wait_ge(bias_staged, 1)
                        nc.vector.tensor_copy(bias_bc[:], stage[0][:, 0:2 * F].rearrange("p (k f) -> p k f", f=F))\
                            .then_inc(bias_ready, 1)

            chunks(dve, layer0)

            def low_part(g):
                dve.wait_ge(stage_act, N_ACT0 + 2 * g + 1)
                nc.vector.tensor_tensor(pos_lo[:, g * TILES:(g + 1) * TILES, :],
                                        stage[g % 2][:].rearrange("p (b f) -> p b f", f=F),
                                        pos_hi[:, g * TILES:(g + 1) * TILES, :].bitcast(f32),
                                        ALU.subtract).then_inc(stage_dve, 1)

            def before_layer1(h):
                if h == 3:
                    residual0(LAST)
                    low_part(0)
                    low_part(1)
                    norm0(LAST, 0)
                    norm0(LAST, 1)
                    norm0(LAST, 2)
                    low_part(2)
                    low_part(3)
                if h in (4, 5):
                    low_part(2 * h - 4)
                    low_part(2 * h - 3)

            def residual1(chunk):
                c, _, parity = chunk
                _, q, half = rows_of(chunk)
                dve.wait_ge(half_used[1], HPC * (c + 1))
                nc.vector.tensor_tensor(sets(z_t), sets(acc[parity]), nodes(feat_t[:], q, half), ALU.add)\
                    .then_inc(acc_read[1], 1)

            def norm1(chunk, part):
                c, q, parity = chunk
                if part == 0:
                    dve.wait_ge(rows_ready, CHUNKS + c + 1)
                    for k in range(TILES):
                        ins = nc.vector.scalar_tensor_tensor(out=y_rows[:, k, :], in0=bias_bc[:, 0, :],
                                                             scalar=diag[:, bass.ds(rows_of(chunk)[0] * TILES + k, 1)],
                                                             in1=to_rows[:, k, :], op0=ALU.mult, op1=ALU.add)
                    ins.then_inc(y_ready, 1)
                    dve.wait_ge(y_ready, c + 1)
                if part == 2 and (not isinstance(c, int) or c > 1):
                    dve.wait_ge(stored[parity], q * 16)
                norm(LN_STEPS * (CHUNKS + c), lambda k: y_rows[:, k, :], lambda k: n_rows[:, parity, k, :],
                     TILES)[part]()

            def last_biases():
                for k in range(TILES):
                    t = rows_of(LAST)[0] * TILES + k
                    ins = nc.vector.tensor_scalar(y_rows[:, k, :], bias_bc[:, 0, :], diag[:, t:t + 1], None, ALU.mult)
                ins.then_inc(y_ready, 1)

            def last_residual(part):
                at, tiles = PARTS[part]
                _, q, half = rows_of(LAST)
                x1 = nodes(feat_t[:], q, half)[:, at * QUARTERS:(at + tiles) * QUARTERS, :]
                z = sets(z_t)[:, at * QUARTERS:(at + tiles) * QUARTERS, :]
                dve.wait_ge(last_summed, part + 1)
                nc.vector.tensor_tensor(z, sets(last_acc[part])[:, 0:tiles * QUARTERS, :], x1, ALU.add)\
                    .then_inc(acc_read[1], 1)

            def last_norm(part):
                at, tiles = PARTS[part]
                y = y_rows[:, at:at + tiles, :]
                dve.wait_ge(rows_ready, 2 * CHUNKS + part)
                dve.wait_ge(y_ready, CHUNKS + part)
                nc.vector.tensor_tensor(y, y, last_rows[part], ALU.add).then_inc(y_ready, 1)
                dve.wait_ge(y_ready, CHUNKS + part + 1)
                if part == 0:
                    dve.wait_ge(stored[LAST[2]], 16 * LAST[1])
                for step in norm(LN_STEPS * (2 * CHUNKS - 1 + part), lambda k: y[:, k, :],
                                 lambda k: n_rows[:, LAST[2], at + k, :], tiles):
                    step()

            def layer1(chunk, before):
                for h in range(HPC):
                    if not before:
                        before_layer1(h)
                    n, hs = turn(1, chunk[0], h)
                    dve.wait_ge(turned[1], n + 1)
                    nc.vector.tensor_scalar(masks[:, hs, :, :], a_cols[:, hs, :, :], 0.0, None, ALU.is_gt)\
                        .then_inc(masked, 1)
                    if h == 3 and before:
                        residual1(before)
                    if h >= 5 and before:
                        norm1(before, h - 5)

            chunks(dve, layer1)

            dve.wait_ge(counted, CHUNKS * PIECES)
            nc.vector.memset(fails[:], 0.0)
            nc.vector.reduce_sum(chunk_signs[:], signs[:].rearrange("p (c s) -> p c s", s=PIECES),
                                 axis=mybir.AxisListType.X).then_inc(stats_step, 1)
            dve.wait_ge(stats_step, 1)
            nc.vector.reduce_sum(fails[:, 1:2], negs[:], axis=mybir.AxisListType.X).then_inc(stats_step, 1)
            dve.wait_ge(stats_pe, 1)
            nc.vector.tensor_scalar(over[0:SQ, :], stage[0][0:SQ, 0:CHUNKS], float(TOP), None, ALU.is_gt)\
                .then_inc(stats_step, 1)
            dve.wait_ge(stats_step, 3)
            nc.vector.reduce_sum(fails[0:SQ, 0:1], over[0:SQ, :], axis=mybir.AxisListType.X).then_inc(stats_step, 1)
            last_biases()
            last_residual(0)
            dve.wait_ge(stats_pe, 2)
            nc.vector.reduce_sum(over[0:1, 0:1], stage[1][0:1, 0:2], axis=mybir.AxisListType.X)\
                .then_inc(stats_step, 1)
            dve.wait_ge(stats_step, 5)
            nc.vector.tensor_scalar(flag[:], over[0:1, 0:1], 0.0, None, ALU.is_gt).then_inc(stats_step, 1)
            last_norm(0)
            last_residual(1)
            last_norm(1)
            dve.wait_ge(normed, NORMS)
            dve.wait_ge(stats_step, 6)
            nc.vector.memset(held_at[:], 0.0).then_inc(flag_ready, 1)

            with when_failed(dve):
                before_layer0(1)

                def held(signal, value):
                    dve.wait_ge(signal, value)
                    nc.vector.memset(held_at[:, 0:1], 0.0)

                nc.vector.memset(top8[:], 0.0).then_inc(g_tile_free, 1)

                def keep_largest(t):
                    base = t * SELECT_STEPS
                    dve.wait_ge(g_loaded[0], t * 32 + 32)
                    nc.vector.scalar_tensor_tensor(out=g_work, in0=g_in, scalar=0.0, in1=g_in, op0=ALU.max,
                                                   op1=ALU.mult).then_inc(g_squared, 1)
                    dve.wait_ge(g_tanh, t + 1)
                    nc.vector.tensor_copy(g_work, g_kept).then_inc(g_select, 1)
                    with dve.Fori(0, ROUNDS) as r:
                        held(g_select, base + r * 2 + 1)
                        nc.vector.max(top8[:], g_work).then_inc(g_select, 1)
                        held(g_select, base + r * 2 + 2)
                        nc.vector.match_replace(out=g_work, in_to_replace=top8[:], in_values=g_work,
                                                imm_value=0.0).then_inc(g_select, 1)
                    done = base + 2 * ROUNDS
                    held(g_select, done + 1)
                    nc.vector.max(top8[:], g_work).then_inc(g_select, 1)
                    held(g_select, done + 2)
                    nc.vector.memset(top8[:, REST:MAX8], 0.0).then_inc(g_select, 1)
                    held(g_select, done + 3)
                    nc.vector.match_replace(out=g_work, in_to_replace=top8[:], in_values=g_work,
                                            imm_value=0.0).then_inc(g_select, 1)
                    dve.wait_ge(g_select, done + 4)
                    nc.vector.tensor_tensor(g_kept, g_kept, g_work, ALU.subtract).then_inc(g_select, 1)
                    held(g_select, done + 5)

                def g_contract(layer, u):
                    rows = g_blk(g_kept if layer == 0 else g_in)
                    nc.vector.memset(g_sum, 0.0).then_inc(g_added, 1)
                    with dve.Fori(0, BLOCKS) as b:
                        n = u * BLOCKS + b
                        nc.vector.tensor_copy(g_pick.rearrange("p (q j) -> p q j", j=SQ), rows[:, b, :, :])\
                            .then_inc(g_picked, 1)
                        dve.wait_ge(g_turned, n + 1)
                        last = nc.vector.tensor_copy(g_cols, stage[0][:, 0:P])
                        if layer == 1:
                            nc.vector.tensor_scalar(g_gt, stage[0][:, 0:P], 0.0, None, ALU.is_gt)
                            last = nc.vector.tensor_scalar(g_lt, stage[0][:, 0:P], 0.0, None, ALU.is_lt)
                        last.then_inc(g_split, 1)
                        dve.wait_ge(g_product, n + 1)
                        dve.wait_ge(g_added, n + u + 1)
                        nc.vector.tensor_tensor(g_sum, g_sum, stage[1][:, 0:F], ALU.add).then_inc(g_added, 1)
                    dve.wait_ge(g_added, (u + 1) * (BLOCKS + 1))

                def g_norm(u):
                    for part in norm((u + NORMS) * LN_STEPS, lambda k: g_y, lambda k: g_out, 1):
                        part()

                def g_layer0(t, q, s):
                    keep_largest(t)
                    g_contract(0, t)
                    nc.vector.tensor_tensor(g_y, g_sum, bias_bc[:, 1, :], ALU.add).then_inc(g_y_step, 1)
                    dve.wait_ge(g_y_step, t * 2 + 1)
                    nc.vector.scalar_tensor_tensor(out=g_y, in0=g_y, scalar=0.0, in1=g_x, op0=ALU.max,
                                                   op1=ALU.add).then_inc(g_y_step, 1)
                    dve.wait_ge(g_y_step, t * 2 + 2)
                    g_norm(t)
                    dve.wait_ge(g_row_turned, t + 1)
                    nc.vector.tensor_copy(g_nodes(q, s), to_cols[:, 0:P].rearrange("f (b j) -> f b j", j=SQ))\
                        .then_inc(g_x1_kept, 1)
                    held(g_x1_kept, t + 1)
                    nc.vector.memset(held_at[:, 1:2], 0.0).then_inc(g_tile_free, 1)

                g_tiles(dve, g_layer0)

                with dve.Fori(0, BLOCKS) as b:
                    nc.vector.tensor_copy(g_pick, feat_t[:, bass.ds(b * P, P)]).then_inc(g_w_picked, 1)
                    dve.wait_ge(g_w_product, b + 1)
                    for k, kept in enumerate((g_pos, g_neg, rhs)):
                        last = nc.vector.tensor_copy(kept[:, b, :], stage[0][:, k * F:(k + 1) * F])
                    last.then_inc(g_w_kept, 1)
                dve.wait_ge(g_w_kept, BLOCKS)

                def g_layer1(t, q, s):
                    dve.wait_ge(g_loaded[1], t * 16 + 16)
                    g_contract(1, t + ALL_TILES)
                    nc.vector.tensor_copy(g_pick.rearrange("f (b j) -> f b j", j=SQ), g_nodes(q, s))\
                        .then_inc(g_x1_picked, 1)
                    dve.wait_ge(g_x1_turned, t + 1)
                    nc.vector.tensor_tensor(g_y, g_sum, to_cols[:, 0:P], ALU.add).then_inc(g_y_step, 1)
                    dve.wait_ge(g_y_step, (t + ALL_TILES) * 2 + 1)
                    nc.vector.scalar_tensor_tensor(out=g_y, in0=bias_bc[:, 0, :], scalar=diag[:, bass.ds(t, 1)],
                                                   in1=g_y, op0=ALU.mult, op1=ALU.add).then_inc(g_y_step, 1)
                    dve.wait_ge(g_y_step, (t + ALL_TILES) * 2 + 2)
                    g_norm(t + ALL_TILES)
                    held(g_stored, t * 16 + 16)
                    nc.vector.memset(held_at[:, 1:2], 0.0).then_inc(g_tile_free, 1)

                g_tiles(dve, g_layer1)

        @block.tensor
        def _(pe):
            pe.wait_ge(consts, 2)
            def before_layer0(run):
                for n, (kind, g) in enumerate(USES):
                    if n >= 4:
                        emptied(pe, n - 4, run)
                    bank = stage[n % 4]
                    if kind == "turn":
                        pe.wait_ge(x_loaded[g], 16 * (run + 1))
                        for k in range(TILES):
                            last = nc.tensor.transpose(bank[:, k * P:(k + 1) * P], xr[:, g * TILES + k, :], ident[:])
                    elif kind == "hid":
                        pe.wait_ge(small_loaded, 64)
                        pe.wait_ge(stage_dve, DVE_EMPTIED[run] + count_of("turn", g))
                        last = nc.tensor.matmul(bank[:], w_pg[:, 0, :], nodes(feat_t[:], g // 2, g % 2),
                                                start=True, stop=True)
                    else:
                        if g in (0, GROUPS // 2):
                            pe.wait_ge(stage_act, ACT_EMPTIED[run] + count_of("hid", GROUPS - 2 if g == 0 else GROUPS - 1))
                        for k in range(TILES):
                            last = nc.tensor.matmul(bank[:, k * P:(k + 1) * P], blk(h_t, g * TILES + k),
                                                    w_pg[:, 1, :], start=True, stop=True)
                    last.then_inc(staged, 1)

            before_layer0(0)
            def turn_to_rows(layer, c):
                if layer == 0:
                    pe.wait_ge(z_ready, c + 1)
                else:
                    pe.wait_ge(acc_read[1], c + 1)
                if layer == 1 or not isinstance(c, int) or c > 0:
                    pe.wait_ge(normed, layer * CHUNKS + c)
                for k in range(TILES):
                    last = nc.tensor.transpose(to_rows[:, k, :], z_t[:, k * P:(k + 1) * P], ident[:])
                last.then_inc(rows_ready, 1)

            def turn_x1_back(chunk):
                c, q, parity = chunk
                pe.wait_ge(normed, c + 1)
                if not isinstance(c, int) or c > 0:
                    pe.wait_ge(x1_ready, c)
                for k in range(TILES):
                    last = nc.tensor.transpose(to_cols[:, k * P:(k + 1) * P], n_rows[:, parity, k, :], ident[:])
                last.then_inc(cols_ready, 1)

            def layer0(chunk, before):
                c, q, parity = chunk
                if not isinstance(c, int) or c > 1:
                    pe.wait_ge(acc_read[0], c - 1)
                for h in range(HPC):
                    n = c * HPC + h
                    if not before:
                        if h < GROUPS // 2:
                            pe.wait_ge(stage_act, count_of("rhs", h))
                        else:
                            pe.wait_ge(stage_dve, count_of("rhs", h))
                    if chunk is LAST and h == 0:
                        pe.wait_ge(wl1_loaded, 96)
                        nc.tensor.matmul(stage[0][:, 0:F], ones[0:1, :], b_row[:, 0, :], start=True, stop=False)
                        nc.tensor.matmul(stage[0][:, 0:F], ones[0:1, :], b_row[:, 1, :], start=False, stop=True)
                        nc.tensor.matmul(stage[0][:, F:2 * F], ones[0:1, :], b_row[:, 2, :], start=True, stop=True)\
                            .then_inc(bias_staged, 1)
                    pe.wait_ge(tanh_done, n + 1)
                    for k in range(HB):
                        b = h * HB + k
                        last = nc.tensor.matmul(acc[parity][:], rhs[:, b, :], a_cols[:, h % HSLOTS, k, :],
                                                start=(b == 0), stop=(b == BLOCKS - 1))
                    last.then_inc(half_used[0], 1)
                    if h == 1 and before:
                        turn_to_rows(0, before[0])
                    if h == 5 and before:
                        turn_x1_back(before)

            chunks(pe, layer0)
            def operands(g):
                if g == 0:
                    pe.wait_ge(x1_ready, CHUNKS - 1)
                    pe.wait_ge(bias_ready, 1)
                if g == PQ // 2:
                    pe.wait_ge(x1_ready, CHUNKS)
                if g >= 2:
                    pe.wait_ge(stage_act, N_ACT0 + 2 * (g - 1))
                    pe.wait_ge(stage_dve, N_DVE0 + g - 1)
                for k in range(TILES):
                    for part, w in ((0, 0), (2, 2)):
                        last = nc.tensor.matmul(stage[part + g % 2][:, k * P:(k + 1) * P],
                                                blk(feat_t[:], g * TILES + k), w_pne[:, w, :],
                                                start=True, stop=True)
                last.then_inc(staged, 1)

            def before_layer1(h):
                if h == 0:
                    operands(0)
                    operands(1)
                    turn_to_rows(0, CHUNKS - 1)
                    operands(2)
                    operands(3)
                if h == 1:
                    turn_x1_back(LAST)
                if h in (2, 3):
                    operands(2 * h)
                    operands(2 * h + 1)
                pe.wait_ge(stage_act, N_ACT0 + 2 * (h + 1))
                pe.wait_ge(stage_dve, N_DVE0 + h + 1)

            def layer1(chunk, before):
                c, q, parity = chunk
                if chunk is LAST:
                    last_chunk()
                    return
                if not isinstance(c, int) or c > 1:
                    pe.wait_ge(acc_read[1], c - 1)
                for h in range(HPC):
                    n = c * HPC + h
                    if not before:
                        before_layer1(h)
                    pe.wait_ge(masked, n + 1)
                    for k in range(HB):
                        b = h * HB + k
                        cols, mask = a_cols[:, h % HSLOTS, k, :], masks[:, h % HSLOTS, k, :]
                        nc.tensor.matmul(acc[parity][:], rhs[:, b, :], cols, start=(b == 0), stop=False)
                        nc.tensor.matmul(acc[parity][:], pos_hi[:, b, :], mask, start=False, stop=False)
                        last = nc.tensor.matmul(acc[parity][:], pos_lo[:, b, :], mask, start=False,
                                                stop=(b == BLOCKS - 1))
                    last.then_inc(half_used[1], 1)
                    if h == 1 and before:
                        turn_to_rows(1, before[0])

            def last_chunk():
                apart = HPC - TOGETHER

                def products(h, part):
                    at, tiles = PARTS[part]
                    for k in range(HB):
                        b = h * HB + k
                        cols = a_cols[:, h % HSLOTS, k, at * P:(at + tiles) * P]
                        mask = masks[:, h % HSLOTS, k, at * P:(at + tiles) * P]
                        sums = last_acc[part][:, 0:tiles * P]
                        nc.tensor.matmul(sums, rhs[:, b, :], cols, start=(b == 0), stop=False)
                        nc.tensor.matmul(sums, pos_hi[:, b, :], mask, start=False, stop=False)
                        last = nc.tensor.matmul(sums, pos_lo[:, b, :], mask, start=False, stop=(b == BLOCKS - 1))
                    return last

                def turned_rows(part):
                    at, tiles = PARTS[part]
                    pe.wait_ge(acc_read[1], CHUNKS + part)
                    if part == 0:
                        pe.wait_ge(normed, 2 * CHUNKS - 1)
                    for k in range(tiles):
                        last = nc.tensor.transpose(last_rows[part][:, k, :], z_t[:, (at + k) * P:(at + k + 1) * P],
                                                   ident[:])
                    last.then_inc(rows_ready, 1)

                pe.wait_ge(acc_read[1], LAST[0] - 1)
                for h in range(apart):
                    pe.wait_ge(masked, LAST[0] * HPC + h + 1)
                    products(h, 0)
                    products(h, 1).then_inc(half_used[1], 1)
                    if h == 1:
                        turn_to_rows(1, LAST[0] - 1)
                for h in range(apart, HPC):
                    pe.wait_ge(masked, LAST[0] * HPC + h + 1)
                    last = products(h, 0)
                last.then_inc(last_summed, 1)
                sum_signs()
                products(apart, 1)
                pe.wait_ge(stats_step, 4)
                nc.tensor.matmul(stage[1][0:1, 0:2], ones[:, 0:1], fails[:], start=True, stop=True).then_inc(stats_pe, 1)
                turned_rows(0)
                for h in range(apart + 1, HPC):
                    last = products(h, 1)
                last.then_inc(last_summed, 1)
                turned_rows(1)

            def sum_signs():
                pe.wait_ge(stats_step, 1)
                for q in range(QUARTERS):
                    last = nc.tensor.matmul(stage[0][0:SQ, 0:CHUNKS], ident[:, q * SQ:(q + 1) * SQ], chunk_signs[:],
                                            start=(q == 0), stop=(q == QUARTERS - 1))
                last.then_inc(stats_pe, 1)

            chunks(pe, layer1)

            with when_failed(pe):
                before_layer0(1)
                pe.wait_ge(stage_dve, DVE_EMPTIED[1] + N_DVE0)
                pe.wait_ge(stage_act, ACT_EMPTIED[1] + N_ACT0)

                def g_contract(layer, u):
                    with pe.Fori(0, BLOCKS) as b:
                        n = u * BLOCKS + b
                        pe.wait_ge(g_picked, n + 1)
                        nc.tensor.transpose(stage[0][:, 0:P], g_pick, ident[:]).then_inc(g_turned, 1)
                        pe.wait_ge(g_split, n + 1)
                        parts = [(g_cols, rhs)] + [(g_gt, g_pos), (g_lt, g_neg)] * layer
                        for k, (cols, operand) in enumerate(parts):
                            last = nc.tensor.matmul(stage[1][:, 0:F], cols, operand[:, b, :], start=(k == 0),
                                                    stop=(k == len(parts) - 1))
                        last.then_inc(g_product, 1)

                def g_layer0(t, q, s):
                    g_contract(0, t)
                    pe.wait_ge(normed, t + NORMS + 1)
                    nc.tensor.transpose(to_cols[:, 0:P], g_out, ident[:]).then_inc(g_row_turned, 1)

                g_tiles(pe, g_layer0)
                with pe.Fori(0, BLOCKS) as b:
                    pe.wait_ge(g_w_picked, b + 1)
                    nc.tensor.matmul(stage[0][:, 0:3 * F], g_pick, w_pne[:].rearrange("p k f -> p (k f)"),
                                     start=True, stop=True).then_inc(g_w_product, 1)

                def g_layer1(t, q, s):
                    g_contract(1, t + ALL_TILES)
                    pe.wait_ge(g_x1_picked, t + 1)
                    nc.tensor.transpose(to_cols[:, 0:P], g_pick, ident[:]).then_inc(g_x1_turned, 1)

                g_tiles(pe, g_layer1)


_INS = ['x', 'adj', 'L0_gnn_W_proj', 'L0_gnn_b_proj', 'L0_gnn_W_gcn', 'L0_gnn_b_gcn', 'L1_gnn_node_weight',
        'L1_gnn_node_bias', 'L1_gnn_edge_weight', 'L1_gnn_edge_bias']


def kernel(**inputs):
    import concourse.bacc as _bacc
    from concourse.bass_utils import run_bass_kernel_spmd as _run

    nc = _bacc.Bacc("TRN2", target_bir_lowering=False, num_devices=1)
    arrays, args = {}, []
    for name in _INS:
        a = np.ascontiguousarray(inputs[name])
        arrays[f"in_{name}_dram"] = a
        args.append(nc.dram_tensor(f"in_{name}_dram", a.shape, mybir.dt.from_np(a.dtype), kind="ExternalInput").ap())
    shape = inputs['x'].shape
    args.append(nc.dram_tensor("out_dram", shape, mybir.dt.float32, kind="ExternalOutput").ap())
    build(nc, *args)
    r = _run(nc, [arrays], core_ids=[0])
    return r.results[0]["out_dram"]
```
